# Optimizing a Trainium2 kernel written in Bass

```python
import numpy as np
import jax
import jax.numpy as jnp

def _softmax(x, axis=-1):
    return jax.nn.softmax(x, axis=axis)

def _gelu(x):
    return jax.nn.gelu(x, approximate=True)

def _silu(x):
    return jax.nn.silu(x)

def _sigmoid(x):
    return jax.nn.sigmoid(x)

def _layernorm(x, axis=-1, eps=1e-05):
    m = jnp.mean(x, axis=axis, keepdims=True)
    v = jnp.var(x, axis=axis, keepdims=True)
    return (x - m) / jnp.sqrt(v + eps)

def _scatter_add(tgt, idx, src, axis=0):
    return tgt.at[idx].add(src)

def _segment_sum(src, seg, n):
    return jax.ops.segment_sum(src, seg, n)
kernel_name = 'mk_adj_preln_d1_adj_r2_2ea263'

def setup_inputs(seed: int=0):
    np.random.seed(seed)
    _w = jnp.asarray

    def _rec_inputs():
        import jax
        import jax.numpy as jnp
        _gk = jax.random.key(seed)
        x = -0.0002928 + 1 * jax.random.normal(jax.random.fold_in(_gk, 1), (128, 128, 1024), jnp.float32)
        _a = jax.random.bernoulli(jax.random.fold_in(_gk, 2), 0.03125, (128, 128))
        _a = jnp.logical_or(_a, jnp.swapaxes(_a, -1, -2))
        _a = jnp.logical_or(_a, jnp.eye(128, dtype=bool))
        _af = _a.astype(jnp.float32)
        _af = _af * jax.random.uniform(jax.random.fold_in(_gk, 3), (128, 128), jnp.float32, 0.05, 0.203735)
        adj = _af
        return (x, adj)
    x, adj = _rec_inputs()

    def _L0_gnn_setup():
        import jax, jax.numpy as jnp
        import numpy as np
        B, C, N = (16, 128, 1024)
        key = jax.random.key(seed)
        ks = jax.random.split(key, 6)
        x = jax.random.normal(ks[0], (B, C, N), jnp.float32)
        wq = jax.random.normal(ks[1], (C // 4, C), jnp.float32) * 0.05
        wv = jax.random.normal(ks[2], (C, C), jnp.float32) * 0.05
        bv = jax.random.normal(ks[3], (C,), jnp.float32) * 0.05
        wt = jax.random.normal(ks[4], (C, C), jnp.float32) * 0.05
        bt = jax.random.normal(ks[5], (C,), jnp.float32) * 0.05
        gamma = jnp.ones((C,), jnp.float32)
        beta = jnp.zeros((C,), jnp.float32)
        bn_mean = jnp.zeros((C,), jnp.float32)
        bn_var = jnp.ones((C,), jnp.float32)
        return dict(x=x, wq=wq, wv=wv, bv=bv, wt=wt, bt=bt, gamma=gamma, beta=beta, bn_mean=bn_mean, bn_var=bn_var)
    _L0_gnn_all = _L0_gnn_setup()
    _L0_gnn_in = {k: v for k, v in _L0_gnn_all.items() if k in ('wq', 'bv', 'bt', 'gamma', 'beta', 'bn_mean', 'bn_var')}
    del _L0_gnn_all
    return {'x': x, 'adj': adj, 'L0_gnn_wq': _L0_gnn_in['wq'], 'L0_gnn_bv': _L0_gnn_in['bv'], 'L0_gnn_bt': _L0_gnn_in['bt'], 'L0_gnn_gamma': _L0_gnn_in['gamma'], 'L0_gnn_beta': _L0_gnn_in['beta'], 'L0_gnn_bn_mean': _L0_gnn_in['bn_mean'], 'L0_gnn_bn_var': _L0_gnn_in['bn_var']}

def reference(x, adj, L0_gnn_wq, L0_gnn_bv, L0_gnn_bt, L0_gnn_gamma, L0_gnn_beta, L0_gnn_bn_mean, L0_gnn_bn_var):
    import jax
    import jax.numpy as jnp

    def _L0_gnn_ref(x, wq, wv, bv, wt, bt, gamma, beta, bn_mean, bn_var):
        import jax, jax.numpy as jnp
        import numpy as np
        B, C, N = (16, 128, 1024)
        EPS = 1e-09
        BN_EPS = 1e-05
        x_q = jnp.einsum('dc,bcn->bnd', wq, x)
        x_k = jnp.einsum('dc,bcn->bdn', wq, x)
        energy = jnp.einsum('bnd,bdm->bnm', x_q, x_k)
        attn = jax.nn.softmax(energy, axis=-1)
        attn = attn / (EPS + attn.sum(axis=1, keepdims=True))
        x_v = jnp.einsum('dc,bcn->bdn', wv, x) + bv[None, :, None]
        x_r = jnp.einsum('bdn,bnm->bdm', x_v, attn)
        t = jnp.einsum('dc,bcn->bdn', wt, x - x_r) + bt[None, :, None]
        t = (t - bn_mean[None, :, None]) * jax.lax.rsqrt(bn_var + BN_EPS)[None, :, None]
        t = t * gamma[None, :, None] + beta[None, :, None]
        return x + jax.nn.relu(t)
    h = jnp.maximum(_layernorm(x, axis=-1), 0.0)
    x = x + _L0_gnn_ref(h, L0_gnn_wq, adj, L0_gnn_bv, adj, L0_gnn_bt, L0_gnn_gamma, L0_gnn_beta, L0_gnn_bn_mean, L0_gnn_bn_var)
    return x

_drawn_inputs = setup_inputs


def setup_inputs(seed=0):
    import zlib

    import numpy as np

    out = dict(_drawn_inputs(seed))
    spreads = {'L0_gnn_gamma': (1.0, 0.6),
     'L0_gnn_beta': (0.0, 0.1),
     'L0_gnn_bn_mean': (0.0, 0.1),
     'L0_gnn_bn_var': (1.0, 0.6)}
    factors = {'L0_gnn_wq': 8.0, 'L0_gnn_bv': 8.0, 'L0_gnn_bt': 2.755}
    for name, (base, spread) in spreads.items():
        noise = np.random.default_rng([zlib.crc32(name.encode()), seed]).standard_normal(out[name].shape)
        drawn = base * np.exp(spread * noise) if base else spread * noise
        out[name] = jnp.asarray(drawn.astype(out[name].dtype))
    for name, factor in factors.items():
        out[name] = (out[name] * factor).astype(out[name].dtype)
    return out
```

```python
from contextlib import ExitStack

import numpy as np

import concourse.bass as bass
from concourse import mybir

ALU = mybir.AluOpType
ACT = mybir.ActivationFunctionType
AX = mybir.AxisListType
F32 = mybir.dt.float32
F16 = mybir.dt.float16
BF16 = mybir.dt.bfloat16
U32 = mybir.dt.uint32

SOFT_EPS = 1e-9
NORM_EPS = 1e-5
EXPONENT_MASK = 0x7F800000


class Frame:

    def __init__(self, c, i, samples, slots):
        self.c, self.i, self.samples, self.slots = c, i, samples, slots
        self.looped = not isinstance(i, int)

    def has(self, d):
        return self.looped or 0 <= self.c + d < self.samples

    def slot(self, d, n):
        return (self.c + d) % n

    def count(self, per, d, more):
        fixed = per * (self.c + d) + more
        return self.i * (per * self.slots) + fixed if self.looped else fixed

    def turn(self, d):
        fixed = (self.c + d) // self.slots + 1
        return self.i + fixed if self.looped else fixed


def gnn_block(nc, x, adj, adj_t, wq_all, wq_t4, bv_rep, prm, consts, out):
    B, C, N = x.shape
    D = wq_t4.shape[1] // 4
    P = 128
    T = N // P
    HALF = N // 2
    HB = T // 2
    SLOTS = 4
    FIRST, LAST = -1, B + 1
    LOOP_FROM = 3
    ROUNDS = (B - 2 - LOOP_FROM) // SLOTS
    LOOP_TO = LOOP_FROM + SLOTS * ROUNDS
    W = P + 1

    with ExitStack() as ctx:
        def sb(name, shape, dt=F32):
            return ctx.enter_context(nc.sbuf_tensor(name, shape, dt))

        def ps(name, cols):
            return ctx.enter_context(nc.psum_tensor(name, [P, cols], F32))

        def sem(name):
            return ctx.enter_context(nc.semaphore(name))

        energy = [ps(f"energy{i}", N) for i in range(2)]
        zpsum = [ps(f"zpsum{i}", HALF) for i in range(2)]
        bank_a = ps("bank_a", HALF)
        bank_b = ps("bank_b", HALF)

        xy = sb("xy", [P, SLOTS, N])
        hid = sb("hid", [P, SLOTS, N])
        q_hi = sb("q_hi", [P, N], F16)
        q_mov = sb("q_mov", [P, 2, N], F16)
        q_sta = sb("q_sta", [P, 2, N], F16)
        prob = sb("prob", [P, 2, T, N])
        ut = sb("ut", [P, 2, T, W])
        zt = sb("zt", [P, 2, T, P])
        act_t = sb("act_t", [P, 2, HALF])
        rowmax = sb("rowmax", [P, T])
        nbias = sb("nbias", [P, T])
        rowsum = sb("rowsum", [P, 2, T])
        den = sb("den", [P, 2])
        inv_den = sb("inv_den", [P, 2])
        stat = sb("stat", [P, 2, 6])
        mv = sb("mv", [P, 2])
        veps = sb("veps", [P, 1])
        zero = sb("zero", [P, 1])
        eps = sb("eps", [P, 1])
        mean_rstd = sb("mean_rstd", [P, 1])
        norm = sb("norm", [P, 2])

        wv_sb = sb("wv_sb", [P, C])
        wt_sb = sb("wt_sb", [P, C])
        wt_bn = sb("wt_bn", [P, C])
        wq_sb = sb("wq_sb", [P, 4 * D])
        wq_sc = sb("wq_sc", [P, 4 * D])
        wq_any = sb("wq_any", [P, D, C])
        bv_sb = sb("bv_sb", [P, P])
        prm_sb = sb("prm_sb", [P, prm.shape[1]])
        con = sb("con", [P, consts.shape[1]])
        g_t = sb("g_t", [P, C])
        inv = sb("inv", [P, P + 1])
        bn_s = sb("bn_s", [P, P + 1])
        bias0 = sb("bias0", [P, 1])
        bias1 = sb("bias1", [P, 1])
        bias = sb("bias", [P, 1])
        neg_half = sb("neg_half", [P, P + 1])
        ones = sb("ones", [P, P], BF16)
        c_hi = sb("c_hi", [P, P], BF16)
        c_mid = sb("c_mid", [P, P], BF16)
        c_lo = sb("c_lo", [P, P], BF16)
        c_r1 = sb("c_r1", [P, P])
        c_r2 = sb("c_r2", [P, P])
        c_s1 = sb("c_s1", [P, P], BF16)
        c_s2 = sb("c_s2", [P, P], BF16)
        c_s3 = sb("c_s3", [P, P], BF16)
        c_rows = sb("c_rows", [P, HB, P], BF16)
        wsum = sb("wsum", [P, D])
        wmax = sb("wmax", [P, 1])
        wclip = sb("wclip", [P, 1])
        pow2 = sb("pow2", [P, 1], U32)
        ipow2 = sb("ipow2", [P, 1])
        alpha = sb("alpha", [P, 1])
        beta = sb("beta", [P, 1])
        nbeta = sb("nbeta", [P, 1])

        ident = con[:, 0:P]
        mask_mov = con[:, P:P + 1]
        mask_sta = con[:, P + 1:P + 2]
        row_mask = [con[:, P + 2 + i:P + 3 + i] for i in range(3)]
        var_p, gamma_p = prm_sb[:, 0:W], prm_sb[:, W:2 * W]
        bt_p, mean_p, beta_p = (prm_sb[:, 2 * W + i:2 * W + i + 1] for i in range(3))

        weights_in = sem("weights_in")
        x_in = [sem(f"x_in{i}") for i in range(SLOTS)]
        y_out = [sem(f"y_out{i}") for i in range(SLOTS)]
        setup_pe = sem("setup_pe")
        energy_done = sem("energy_done")
        z_done = sem("z_done")
        q_done = sem("q_done")
        u_done = sem("u_done")
        t_done = sem("t_done")
        setup_dve = sem("setup_dve")
        max_done = sem("max_done")
        nbias_done = sem("nbias_done")
        split_done = sem("split_done")
        inv_done = sem("inv_done")
        ut_done = sem("ut_done")
        den_done = sem("den_done")
        inv_den_done = sem("inv_den_done")
        stat_step = sem("stat_step")
        stats_done = sem("stats_done")
        prob_done = sem("prob_done")
        qhi_done = sem("qhi_done")
        hid_done = sem("hid_done")
        relu_done = sem("relu_done")
        zt_done = sem("zt_done")
        setup_pool = sem("setup_pool")
        norm_step = sem("norm_step")
        norm_done = sem("norm_done")
        xh_done = sem("xh_done")
        y_done = sem("y_done")

        BN_DONE = 10
        DVE_READY = 20

        block = ctx.enter_context(nc.Block())

        def frames(eng, frame):
            for c in range(FIRST, LOOP_FROM):
                frame(Frame(c, 0, B, SLOTS))
            with eng.Fori(0, ROUNDS) as i:
                for j in range(SLOTS):
                    frame(Frame(LOOP_FROM + j, i, B, SLOTS))
            for c in range(LOOP_TO, LAST + 1):
                frame(Frame(c, 0, B, SLOTS))

        @block.sync
        def _(sp):
            loads = [(con[:, :], consts), (prm_sb[:, :], prm), (wv_sb[:, :], adj), (wt_sb[:, :], adj_t),
                     (wq_sb[:, :], wq_t4), (bv_sb[:, :], bv_rep), (wq_any[:, :, :], wq_all)]
            for b in range(2):
                sp.dma_start(xy[:, b, :], x[b]).then_inc(x_in[b], 16)
            for dst, src in loads:
                sp.dma_start(dst, src).then_inc(weights_in, 16)
            for b in range(2, SLOTS):
                sp.dma_start(xy[:, b, :], x[b]).then_inc(x_in[b], 16)

            def frame(f):
                if f.has(-2):
                    s = f.slot(-2, SLOTS)
                    sp.wait_ge(y_done, f.count(2, -2, 2))
                    row = f.count(1, -2, 0)
                    sp.dma_start(out[row] if isinstance(row, int) else
                                 out[bass.ds(row, 1)].rearrange("a c n -> (a c) n"),
                                 xy[:, s, :]).then_inc(y_out[s], 16)
                    if f.has(2):
                        sp.wait_ge(y_out[s], f.turn(-2) * 16)
                        row = f.count(1, 2, 0)
                        sp.dma_start(xy[:, s, :], x[row] if isinstance(row, int) else
                                     x[bass.ds(row, 1)].rearrange("a c n -> (a c) n")).then_inc(x_in[s], 16)

            frames(sp, frame)
            for s in range(SLOTS):
                sp.wait_ge(y_out[s], 16 * (B // SLOTS))

        @block.tensor
        def _(pe):
            pe.wait_ge(weights_in, 16 * 7)
            pe.wait_ge(setup_pool, BN_DONE)
            pe.matmul(bank_a[:, 0:P], wv_sb[:, :], wt_bn[:, :], start=True, stop=True).then_inc(setup_pe, 1)
            pe.matmul(bank_b[:, 0:P], bv_sb[:, :], wt_bn[:, :], start=True, stop=True).then_inc(setup_pe, 1)
            pe.wait_ge(setup_dve, DVE_READY)

            def energies(f, k):
                if not f.has(0):
                    return
                if k == 0:
                    pe.wait_ge(split_done, f.count(2, 0, 2))
                if k >= 2 or f.has(-1):
                    pe.wait_ge(prob_done, f.count(T, 0, k - 1))
                b = f.slot(0, 2)
                for g in range(2):
                    mm = pe.matmul(energy[k % 2][:, g * HALF:(g + 1) * HALF], q_sta[:, b, k * P:(k + 1) * P],
                                   q_mov[:, b, g * HALF:(g + 1) * HALF], start=True, stop=True)
                mm.then_inc(energy_done, 1)

            def attend(f, k):
                d, m = (-1, k - 1) if k else (-2, T - 1)
                if not f.has(d):
                    return
                if m == 0:
                    pe.wait_ge(ut_done, f.count(2, d, 2))
                if m >= 2 or f.has(d - 1):
                    pe.wait_ge(zt_done, f.count(T, d, m - 1))
                b = f.slot(d, 2)
                for n in range(T):
                    mm = pe.matmul(zpsum[m % 2][:, 0:W], prob[:, b, n, m * P:(m + 1) * P], ut[:, b, n, :],
                                   start=(n == 0), stop=(n == T - 1))
                mm.then_inc(z_done, 1)

            def project_q(f, g):
                if not f.has(1):
                    return
                if g == 0:
                    pe.wait_ge(hid_done, f.count(1, 1, 1))
                    if f.has(-1):
                        pe.wait_ge(ut_done, f.count(2, 0, 0))
                else:
                    if f.has(-2):
                        pe.wait_ge(relu_done, f.count(2, -2, 2))
                bank = bank_a if g else bank_b
                pe.matmul(bank[:, :], wq_sc[:, :], hid[:, f.slot(1, SLOTS), g * HALF:(g + 1) * HALF],
                          start=True, stop=True).then_inc(q_done, 1)

            def project_u(f, g):
                if not f.has(0):
                    return
                if g == 0:
                    if f.has(1):
                        pe.wait_ge(split_done, f.count(2, 1, 1))
                    else:
                        pe.wait_ge(ut_done, f.count(2, 0, 0))
                else:
                    pe.wait_ge(ut_done, f.count(2, 0, 1))
                pe.matmul(bank_b[:, :], ones[:, :], c_rows[:, :, :], start=True, stop=False)
                for j in range(HB):
                    n = g * HB + j
                    mm = pe.matmul(bank_b[:, j * P:(j + 1) * P], hid[:, f.slot(0, SLOTS), n * P:(n + 1) * P],
                                   g_t[:, :], start=False, stop=(j == HB - 1))
                mm.then_inc(u_done, 1)

            def transform(f, g):
                d = -2 if g else -1
                if not f.has(d):
                    return
                if g:
                    pe.wait_ge(relu_done, f.count(2, d, 1))
                elif f.has(1):
                    pe.wait_ge(split_done, f.count(2, 1, 2))
                else:
                    if f.has(-2):
                        pe.wait_ge(relu_done, f.count(2, -2, 2))
                pe.wait_ge(zt_done, f.count(T, d, (g + 1) * HB))
                pe.matmul(bank_a[:, :], wt_bn[:, :], hid[:, f.slot(d, SLOTS), g * HALF:(g + 1) * HALF],
                          start=True, stop=False)
                for j in range(HB):
                    mm = pe.matmul(bank_a[:, j * P:(j + 1) * P], zt[:, f.slot(d, 2), g * HB + j, :], ident,
                                   start=False, stop=(j == HB - 1), is_transpose=True)
                mm.then_inc(t_done, 1)

            def frame(f):
                for k in range(T):
                    energies(f, k)
                    attend(f, k)
                    if k == 2:
                        transform(f, 1)
                    elif k == 3:
                        project_q(f, 0)
                    elif k == 4:
                        project_q(f, 1)
                    elif k == 5:
                        project_u(f, 0)
                    elif k == 6:
                        transform(f, 0)
                    elif k == 7:
                        project_u(f, 1)

            frames(pe, frame)

        @block.vector
        def _(dve):
            steps = [0]

            def step(ins):
                steps[0] += 1
                ins.then_inc(setup_dve, 1)
                dve.wait_ge(setup_dve, steps[0])

            step(dve.memset(ones[:, :], 1.0))
            dve.wait_ge(weights_in, 16 * 7)
            step(dve.tensor_reduce(wsum[:, :], wq_any[:, :, :], AX.X, ALU.add, apply_absolute_value=True))
            step(dve.tensor_reduce(wmax[:, :], wsum[:, :], AX.X, ALU.max))
            step(dve.tensor_scalar(wclip[:, :], wmax[:, :], 2.0 ** -40, 2.0 ** 40, ALU.max, ALU.min))
            step(dve.tensor_scalar(pow2[:, :], wclip[:, :].bitcast(U32), EXPONENT_MASK, None, ALU.bitwise_and))
            step(dve.reciprocal(ipow2[:, :], pow2[:, :].bitcast(F32)))
            step(dve.tensor_scalar(alpha[:, :], ipow2[:, :], 2.0 ** 9, None, ALU.mult))
            step(dve.tensor_scalar(beta[:, :], pow2[:, :].bitcast(F32), pow2[:, :].bitcast(F32), 2.0 ** -18,
                                   ALU.mult, ALU.mult))
            step(dve.tensor_scalar(nbeta[:, :], beta[:, :], -1.0, None, ALU.mult))
            step(dve.tensor_scalar(wq_sc[:, :], wq_sb[:, :], alpha[:, :], None, ALU.mult))
            dve.wait_ge(setup_pe, 2)
            step(dve.tensor_copy(g_t[:, :], bank_a[:, 0:P]))
            step(dve.tensor_copy(c_hi[:, :], bank_b[:, 0:P]))
            step(dve.tensor_tensor(c_r1[:, :], bank_b[:, 0:P], c_hi[:, :], ALU.subtract))
            step(dve.tensor_copy(c_mid[:, :], c_r1[:, :]))
            step(dve.tensor_tensor(c_r2[:, :], c_r1[:, :], c_mid[:, :], ALU.subtract))
            step(dve.tensor_copy(c_lo[:, :], c_r2[:, :]))
            step(dve.tensor_scalar(c_s1[:, :], c_hi[:, :], row_mask[0], None, ALU.mult))
            step(dve.scalar_tensor_tensor(c_s2[:, :], c_mid[:, :], row_mask[1], c_s1[:, :], ALU.mult, ALU.add))
            step(dve.scalar_tensor_tensor(c_s3[:, :], c_lo[:, :], row_mask[2], c_s2[:, :], ALU.mult, ALU.add))
            step(dve.tensor_copy(c_rows[:, :, :], c_s3[:, None, :].to_broadcast([P, HB, P])))
            assert steps[0] == DVE_READY, steps

            def row_max(f, k):
                if not f.has(0):
                    return
                dve.wait_ge(energy_done, f.count(T, 0, k + 1))
                dve.tensor_reduce(rowmax[:, k:k + 1], energy[k % 2][:, :], AX.X, ALU.max).then_inc(max_done, 1)
                dve.wait_ge(max_done, f.count(T, 0, k + 1))
                dve.tensor_scalar(nbias[:, k:k + 1], rowmax[:, k:k + 1], nbeta[:, :], None,
                                  ALU.mult).then_inc(nbias_done, 1)

            def invert_colsum(f, k):
                d, m = (-1, k - 2) if k >= 2 else (-2, T - 2 + k)
                if not f.has(d):
                    return
                dve.wait_ge(z_done, f.count(T, d, m + 1))
                dve.tensor_scalar(den[:, m % 2:m % 2 + 1], zpsum[m % 2][:, P:W], SOFT_EPS, -1.0, ALU.add,
                                  ALU.mult).then_inc(den_done, 1)
                dve.wait_ge(den_done, f.count(T, d, m + 1))
                dve.reciprocal(inv_den[:, m % 2:m % 2 + 1], den[:, m % 2:m % 2 + 1]).then_inc(inv_den_done, 1)

            def scale_u(f, g):
                d = -1 if g else 0
                if not f.has(d):
                    return
                b = f.slot(d, 2)
                blocks = slice(g * HB, (g + 1) * HB)
                dve.wait_ge(prob_done, f.count(T, d, (g + 1) * HB))
                dve.reciprocal(ut[:, b, blocks, P:W], rowsum[:, b, blocks].rearrange("p (t a) -> p t a", a=1)
                               ).then_inc(inv_done, 1)
                dve.wait_ge(inv_done, f.count(2, d, g + 1))
                dve.wait_ge(u_done, f.count(2, d, g + 1))
                dve.tensor_tensor(ut[:, b, blocks, 0:P], bank_b[:, :].rearrange("p (t c) -> p t c", c=P),
                                  ut[:, b, blocks, P:W].to_broadcast([P, HB, P]), ALU.mult).then_inc(ut_done, 1)

            def split_q(f, g):
                if not f.has(1):
                    return
                b = f.slot(1, 2)
                half = slice(g * HALF, (g + 1) * HALF)
                bank = bank_a if g else bank_b
                dve.wait_ge(qhi_done, f.count(2, 1, g + 1))
                dve.scalar_tensor_tensor(q_mov[:, b, half], q_hi[:, half], mask_mov, bank[:, :], ALU.mult, ALU.add)
                dve.scalar_tensor_tensor(q_sta[:, b, half], q_hi[:, half], mask_sta, bank[:, :], ALU.mult,
                                         ALU.add).then_inc(split_done, 1)

            def stats(f):
                if not f.has(1):
                    return
                s = f.slot(1, SLOTS)
                dve.wait_ge(x_in[s], f.turn(1) * 16)
                for g in range(2):
                    dve.bn_stats(stat[:, g, :], xy[:, s, g * HALF:(g + 1) * HALF]).then_inc(stat_step, 1)

            def await_stats(f):
                if not f.has(1):
                    return
                dve.wait_ge(stat_step, f.count(2, 1, 2))
                if f.has(0):
                    dve.wait_ge(norm_done, f.count(1, 1, 0))

            def aggregate(f):
                if not f.has(1):
                    return
                dve.bn_aggr(mv[:, :], stat[:, :, :]).then_inc(stats_done, 1)

            def frame(f):
                for k in range(T):
                    invert_colsum(f, k)
                    if k == 1:
                        await_stats(f)
                    row_max(f, k)
                    if k == 0:
                        scale_u(f, 1)
                        stats(f)
                    elif k == 1:
                        aggregate(f)
                    elif k == 4:
                        split_q(f, 0)
                    elif k == 5:
                        split_q(f, 1)
                    elif k == 6:
                        scale_u(f, 0)

            frames(dve, frame)

        @block.scalar
        def _(act):
            act.wait_ge(setup_dve, DVE_READY)
            act.wait_ge(setup_pool, BN_DONE)

            def softmax(f, k):
                if not f.has(0):
                    return
                if k == 0 and f.has(-2):
                    act.wait_ge(z_done, f.count(T, -1, 0))
                act.wait_ge(nbias_done, f.count(T, 0, k + 1))
                b = f.slot(0, 2)
                act.activation(prob[:, b, k, :], energy[k % 2][:, :], ACT.Exp, bias=nbias[:, k:k + 1],
                               scale=beta[:, :], accum_out=rowsum[:, b, k:k + 1]).then_inc(prob_done, 1)

            def hidden(f):
                if not f.has(1):
                    return
                s = f.slot(1, SLOTS)
                act.wait_ge(norm_done, f.count(1, 1, 1))
                if f.has(-3):
                    act.wait_ge(t_done, f.count(2, -3, 2))
                act.activation(hid[:, s, :], xy[:, s, :], ACT.Relu, bias=norm[:, 1:2],
                               scale=norm[:, 0:1]).then_inc(hid_done, 1)

            def high_q(f, g):
                if not f.has(1):
                    return
                half = slice(g * HALF, (g + 1) * HALF)
                act.wait_ge(q_done, f.count(2, 1, g + 1))
                if f.has(0):
                    act.wait_ge(split_done, f.count(2, 0, g + 1))
                act.activation(q_hi[:, half], (bank_a if g else bank_b)[:, :], ACT.Copy).then_inc(qhi_done, 1)

            def relu(f, g):
                d = -2 if g else -1
                if not f.has(d):
                    return
                act.wait_ge(t_done, f.count(2, d, g + 1))
                if f.has(d - 1):
                    act.wait_ge(y_done, f.count(2, d, g - 1))
                act.activation(act_t[:, g, :], bank_a[:, :], ACT.Relu, bias=bias[:, :]).then_inc(relu_done, 1)

            def scale_z(f, k):
                d, m = (-1, k - 2) if k >= 2 else (-2, T - 2 + k)
                if not f.has(d):
                    return
                act.wait_ge(inv_den_done, f.count(T, d, m + 1))
                if m == 0 and f.has(d - 2):
                    act.wait_ge(t_done, f.count(2, d, -2))
                act.activation(zt[:, f.slot(d, 2), m, :], zpsum[m % 2][:, 0:P], ACT.Copy,
                               scale=inv_den[:, m % 2:m % 2 + 1]).then_inc(zt_done, 1)

            def frame(f):
                for k in range(T):
                    scale_z(f, k)
                    if k == 3:
                        relu(f, 1)
                    elif k == 4:
                        high_q(f, 0)
                    elif k == 5:
                        high_q(f, 1)
                    elif k == 7:
                        relu(f, 0)
                    softmax(f, k)
                    if k == 1:
                        hidden(f)

            frames(act, frame)

        @block.gpsimd
        def _(pool):
            steps = [0]

            def step(ins):
                steps[0] += 1
                ins.then_inc(setup_pool, 1)
                pool.wait_ge(setup_pool, steps[0])

            step(pool.memset(neg_half[:, :], -0.5))
            pool.wait_ge(weights_in, 16 * 7)
            step(pool.tensor_scalar(inv[:, :], var_p, NORM_EPS, None, ALU.add))
            step(pool.tensor_tensor(bn_s[:, :], inv[:, :], neg_half[:, :], ALU.pow))
            step(pool.tensor_tensor(inv[:, :], bn_s[:, :], gamma_p, ALU.mult))
            step(pool.tensor_tensor(wt_bn[:, :], wt_sb[:, :], inv[:, 0:P], ALU.mult))
            step(pool.tensor_tensor(bias0[:, :], bt_p, mean_p, ALU.subtract))
            step(pool.tensor_tensor(bias1[:, :], bias0[:, :], inv[:, P:W], ALU.mult))
            step(pool.tensor_tensor(bias[:, :], bias1[:, :], beta_p, ALU.add))
            step(pool.memset(zero[:, :], 0.0))
            step(pool.memset(eps[:, :], NORM_EPS))
            assert steps[0] == BN_DONE

            def layer_norm(f):
                if not f.has(1):
                    return
                pool.wait_ge(stats_done, f.count(1, 1, 1))
                pool.tensor_tensor(veps[:, :], mv[:, 1:2], eps[:, :], ALU.add).then_inc(norm_step, 1)
                pool.wait_ge(norm_step, f.count(3, 1, 1))
                if f.has(0):
                    pool.wait_ge(hid_done, f.count(1, 1, 0))
                pool.tensor_tensor(norm[:, 0:1], veps[:, :], neg_half[:, 0:1], ALU.pow).then_inc(norm_step, 1)
                pool.wait_ge(norm_step, f.count(3, 1, 2))
                pool.tensor_tensor(mean_rstd[:, :], mv[:, 0:1], norm[:, 0:1], ALU.mult).then_inc(norm_step, 1)
                pool.wait_ge(norm_step, f.count(3, 1, 3))
                pool.tensor_tensor(norm[:, 1:2], zero[:, :], mean_rstd[:, :], ALU.subtract).then_inc(norm_done, 1)

            def add_hidden(f):
                if not f.has(1):
                    return
                s = f.slot(1, SLOTS)
                pool.wait_ge(hid_done, f.count(1, 1, 1))
                pool.tensor_tensor(xy[:, s, :], xy[:, s, :], hid[:, s, :], ALU.add).then_inc(xh_done, 1)

            def finish(f, g):
                d = -2 if g else -1
                if not f.has(d):
                    return
                s = f.slot(d, SLOTS)
                half = slice(g * HALF, (g + 1) * HALF)
                pool.wait_ge(relu_done, f.count(2, d, g + 1))
                pool.wait_ge(xh_done, f.count(1, d, 1))
                pool.tensor_tensor(xy[:, s, half], xy[:, s, half], act_t[:, g, :], ALU.add).then_inc(y_done, 1)

            def frame(f):
                layer_norm(f)
                add_hidden(f)
                finish(f, 1)
                finish(f, 0)

            frames(pool, frame)


def kernel(x, adj, L0_gnn_wq, L0_gnn_bv, L0_gnn_bt, L0_gnn_gamma, L0_gnn_beta, L0_gnn_bn_mean, L0_gnn_bn_var):
    import concourse.bacc as _bacc
    from concourse.bass_utils import run_bass_kernel_spmd as _run

    P = 128
    x, adj, wq = np.asarray(x), np.asarray(adj), np.asarray(L0_gnn_wq)
    bv, bt = np.asarray(L0_gnn_bv), np.asarray(L0_gnn_bt)
    gamma, beta = np.asarray(L0_gnn_gamma), np.asarray(L0_gnn_beta)
    mean, var = np.asarray(L0_gnn_bn_mean), np.asarray(L0_gnn_bn_var)
    D, C = wq.shape

    def as_rows(v):
        return np.broadcast_to(v[None, :], (P, C))

    consts = np.zeros((P, P + 5), np.float32)
    consts[:, 0:P] = np.eye(P, dtype=np.float32)
    group = np.arange(P) // D
    consts[:, P] = np.where(group >= 2, -1.0, 0.0)
    consts[:, P + 1] = np.where(group % 2 == 1, -1.0, 0.0)
    consts[0:3, P + 2:P + 5] = np.eye(3, dtype=np.float32)

    arrays = {
        "x": x,
        "adj": adj,
        "adj_t": np.ascontiguousarray(adj.T),
        "wq_all": np.ascontiguousarray(np.broadcast_to(wq[None], (P, D, C))),
        "wq_t4": np.ascontiguousarray(np.concatenate([wq.T] * 4, axis=1)),
        "bv_rep": np.ascontiguousarray(np.broadcast_to(bv[:, None], (C, P))),
        "prm": np.ascontiguousarray(np.concatenate(
            [as_rows(var), var[:, None], as_rows(gamma), gamma[:, None], bt[:, None], mean[:, None], beta[:, None]],
            axis=1)),
        "consts": consts,
    }
    nc = _bacc.Bacc("TRN2", target_bir_lowering=False, num_devices=1)
    args = [nc.dram_tensor(f"in_{n}", a.shape, mybir.dt.from_np(a.dtype), kind="ExternalInput").ap()
            for n, a in arrays.items()]
    args.append(nc.dram_tensor("out_y", x.shape, mybir.dt.float32, kind="ExternalOutput").ap())
    gnn_block(nc, *args)
    r = _run(nc, [{f"in_{n}": a for n, a in arrays.items()}], core_ids=[0])
    return r.results[0]["out_y"]
```

```python
from contextlib import ExitStack

import numpy as np

import concourse.bass as bass
from concourse import mybir

ALU = mybir.AluOpType
ACT = mybir.ActivationFunctionType
AX = mybir.AxisListType
F32 = mybir.dt.float32
F16 = mybir.dt.float16
U32 = mybir.dt.uint32

SOFT_EPS = 1e-9
NORM_EPS = 1e-5
EXPONENT_MASK = 0x7F800000


class Frame:

    def __init__(self, c, i, samples, slots):
        self.c, self.i, self.samples, self.slots = c, i, samples, slots
        self.looped = not isinstance(i, int)

    def has(self, d):
        return self.looped or 0 <= self.c + d < self.samples

    def slot(self, d, n):
        return (self.c + d) % n

    def count(self, per, d, more):
        fixed = per * (self.c + d) + more
        return self.i * (per * self.slots) + fixed if self.looped else fixed

    def turn(self, d):
        fixed = (self.c + d) // self.slots + 1
        return self.i + fixed if self.looped else fixed


def gnn_block(nc, x, adj, adj_t, wq_t4, bv_rep, prm, consts, out):
    B, C, N = x.shape
    D = wq_t4.shape[1] // 4
    P = 128
    T = N // P
    HALF = N // 2
    HB = T // 2
    SLOTS = 4
    FIRST, LAST = -1, B + 1
    LOOP_FROM = 3
    ROUNDS = (B - 2 - LOOP_FROM) // SLOTS
    LOOP_TO = LOOP_FROM + SLOTS * ROUNDS
    W = P + 1

    with ExitStack() as ctx:
        def sb(name, shape, dt=F32):
            return ctx.enter_context(nc.sbuf_tensor(name, shape, dt))

        def ps(name, cols):
            return ctx.enter_context(nc.psum_tensor(name, [P, cols], F32))

        def sem(name):
            return ctx.enter_context(nc.semaphore(name))

        energy = [ps(f"energy{i}", N) for i in range(2)]
        zpsum = [ps(f"zpsum{i}", HALF) for i in range(2)]
        bank_a = ps("bank_a", HALF)
        bank_b = ps("bank_b", HALF)

        x_sb = sb("x_sb", [P, SLOTS, N])
        xhy = sb("xhy", [P, SLOTS, N])
        hid = sb("hid", [P, 2, N])
        hid_hi = sb("hid_hi", [P, SLOTS, N], F16)
        hid_lo = sb("hid_lo", [P, SLOTS, N], F16)
        q_hi = sb("q_hi", [P, N], F16)
        q_mov = sb("q_mov", [P, 2, N], F16)
        q_sta = sb("q_sta", [P, 2, N], F16)
        prob = sb("prob", [P, 2, T, N])
        u_raw = sb("u_raw", [P, T, P])
        ut = sb("ut", [P, 2, T, W])
        zt = sb("zt", [P, 2, T, P])
        act_t = sb("act_t", [P, 2, HALF])
        rowmax = sb("rowmax", [P, T])
        nbias = sb("nbias", [P, T])
        rowsum = sb("rowsum", [P, 2, T])
        den = sb("den", [P, 2, 2, 1])
        inv_den = sb("inv_den", [P, 2, 2, 1])
        stat = sb("stat", [P, 2, 6])
        mv = sb("mv", [P, 2])
        veps = sb("veps", [P, 1])
        mean_rstd = sb("mean_rstd", [P, 1])
        norm = sb("norm", [P, 2, 2])

        con = sb("con", [P, consts.shape[1]])
        prm_sb = sb("prm_sb", [P, prm.shape[1]])
        wv_sb = sb("wv_sb", [P, C])
        wt_sb = sb("wt_sb", [P, C])
        wq_sb = sb("wq_sb", [P, 4 * D])
        bv_sb = sb("bv_sb", [P, P])
        absmax = sb("absmax", [P, 2])
        allmax = sb("allmax", [P, 2])
        clipped = sb("clipped", [P, 2])
        pow2 = sb("pow2", [P, 2], U32)
        ipow2 = sb("ipow2", [P, 2])
        lam = sb("lam", [P, 1])
        mu = sb("mu", [P, 1])
        neg_mu = sb("neg_mu", [P, 1])
        alpha = sb("alpha", [P, 1])
        beta = sb("beta", [P, 1])
        nbeta = sb("nbeta", [P, 1])
        wt_f32 = sb("wt_f32", [P, C])
        wt_hi = sb("wt_hi", [P, C], F16)
        wt_lo = sb("wt_lo", [P, C], F16)
        wq_f32 = sb("wq_f32", [P, 4 * D])
        wq_hi = sb("wq_hi", [P, 4 * D], F16)
        wq_lo = sb("wq_lo", [P, 4 * D], F16)
        g_f32 = sb("g_f32", [P, C])
        g_hi = sb("g_hi", [P, C], F16)
        g_lo = sb("g_lo", [P, C], F16)
        c_row = sb("c_row", [P, C])
        neg_half = sb("neg_half", [P, 1])
        zero = sb("zero", [P, 1])
        warm = sb("warm", [P, 1])
        eps = sb("eps", [P, 1])
        bn_var = sb("bn_var", [P, 1])
        bn_inv = sb("bn_inv", [P, 1])
        bn_scale = sb("bn_scale", [P, 1])
        bias0 = sb("bias0", [P, 1])
        bias1 = sb("bias1", [P, 1])
        bias = sb("bias", [P, 1])
        t_scale = sb("t_scale", [P, 1])

        ident = con[:, 0:P]
        mask_mov = con[:, P:P + 1]
        mask_sta = con[:, P + 1:P + 2]
        var_p, gamma_p, bt_p, mean_p, beta_p = (prm_sb[:, i:i + 1] for i in range(5))

        weights_in = sem("weights_in")
        x_in = [sem(f"x_in{i}") for i in range(SLOTS)]
        y_out = [sem(f"y_out{i}") for i in range(SLOTS)]
        setup_pe = sem("setup_pe")
        energy_done = sem("energy_done")
        z_done = sem("z_done")
        q_done = sem("q_done")
        u_done = sem("u_done")
        t_done = sem("t_done")
        setup_dve = sem("setup_dve")
        max_done = sem("max_done")
        nbias_done = sem("nbias_done")
        split_done = sem("split_done")
        inv_done = sem("inv_done")
        u_raw_done = sem("u_raw_done")
        den_done = sem("den_done")
        inv_den_done = sem("inv_den_done")
        stat_step = sem("stat_step")
        stats_done = sem("stats_done")
        prob_done = sem("prob_done")
        qhi_done = sem("qhi_done")
        hid_done = sem("hid_done")
        relu_done = sem("relu_done")
        zt_done = sem("zt_done")
        setup_pool = sem("setup_pool")
        norm_step = sem("norm_step")
        norm_done = sem("norm_done")
        hid_lo_done = sem("hid_lo_done")
        ut_done = sem("ut_done")
        xh_done = sem("xh_done")
        y_done = sem("y_done")

        MAX_DONE = 4
        BN_DONE = 10
        WT_DONE = 14
        DVE_READY = 22
        WEIGHTS = 6

        block = ctx.enter_context(nc.Block())

        def frames(eng, frame):
            for c in range(FIRST, LOOP_FROM):
                frame(Frame(c, 0, B, SLOTS))
            with eng.Fori(0, ROUNDS) as i:
                for j in range(SLOTS):
                    frame(Frame(LOOP_FROM + j, i, B, SLOTS))
            for c in range(LOOP_TO, LAST + 1):
                frame(Frame(c, 0, B, SLOTS))

        @block.sync
        def _(sp):
            loads = [(wv_sb[:, :], adj), (wq_sb[:, :], wq_t4), (wt_sb[:, :], adj_t), (bv_sb[:, :], bv_rep),
                     (prm_sb[:, :], prm), (con[:, :], consts)]
            assert len(loads) == WEIGHTS
            for dst, src in loads[:4]:
                sp.dma_start(dst, src).then_inc(weights_in, 16)
            sp.dma_start(x_sb[:, 0, :], x[0]).then_inc(x_in[0], 16)
            for dst, src in loads[4:]:
                sp.dma_start(dst, src).then_inc(weights_in, 16)
            for b in range(1, SLOTS):
                sp.dma_start(x_sb[:, b, :], x[b]).then_inc(x_in[b], 16)

            def sample(tensor, row):
                return tensor[row] if isinstance(row, int) else \
                    tensor[bass.ds(row, 1)].rearrange("a c n -> (a c) n")

            def frame(f):
                if f.has(0) and f.has(4):
                    s = f.slot(0, SLOTS)
                    sp.wait_ge(xh_done, f.count(1, 0, 1))
                    sp.dma_start(x_sb[:, s, :], sample(x, f.count(1, 4, 0))).then_inc(x_in[s], 16)
                if f.has(-2):
                    s = f.slot(-2, SLOTS)
                    sp.wait_ge(y_done, f.count(2, -2, 2))
                    sp.dma_start(sample(out, f.count(1, -2, 0)), xhy[:, s, :]).then_inc(y_out[s], 16)

            frames(sp, frame)
            for s in range(SLOTS):
                sp.wait_ge(y_out[s], 16 * (B // SLOTS))

        @block.tensor
        def _(pe):
            pe.wait_ge(weights_in, 16 * WEIGHTS)
            pe.wait_ge(setup_dve, WT_DONE)
            pe.matmul(bank_a[:, 0:P], wv_sb[:, :], wt_f32[:, :], start=True, stop=True).then_inc(setup_pe, 1)
            pe.matmul(bank_b[:, 0:P], bv_sb[:, :], wt_f32[:, :], start=True, stop=True).then_inc(setup_pe, 1)
            pe.wait_ge(setup_dve, DVE_READY)

            def energies(f, k):
                if not f.has(0):
                    return
                if k == 0:
                    pe.wait_ge(split_done, f.count(2, 0, 2))
                if k >= 2 or f.has(-1):
                    pe.wait_ge(prob_done, f.count(T, 0, k - 1))
                b = f.slot(0, 2)
                for g in range(2):
                    mm = pe.matmul(energy[k % 2][:, g * HALF:(g + 1) * HALF], q_sta[:, b, k * P:(k + 1) * P],
                                   q_mov[:, b, g * HALF:(g + 1) * HALF], start=True, stop=True)
                mm.then_inc(energy_done, 1)

            def attend(f, k):
                d, m = (-1, k - 1) if k else (-2, T - 1)
                if not f.has(d):
                    return
                if m % 2 == 0 and (m >= 4 or f.has(d - 1)):
                    pe.wait_ge(zt_done, f.count(T, d, m - 2))
                b = f.slot(d, 2)
                z = zpsum[m // 2 % 2][:, m % 2 * W:(m % 2 + 1) * W]
                for n in range(T):
                    if m == 0 and n % HB == 0:
                        pe.wait_ge(ut_done, f.count(2, d, n // HB + 1))
                    mm = pe.matmul(z, prob[:, b, n, m * P:(m + 1) * P], ut[:, b, n, :],
                                   start=(n == 0), stop=(n == T - 1))
                mm.then_inc(z_done, 1)

            def project_q(f, g):
                if not f.has(1):
                    return
                pe.wait_ge(hid_lo_done, f.count(2, 1, g + 1))
                if g == 0:
                    if f.has(-1):
                        pe.wait_ge(u_raw_done, f.count(2, 0, 0))
                else:
                    if f.has(-2):
                        pe.wait_ge(relu_done, f.count(2, -2, 2))
                bank = bank_a if g else bank_b
                s, half = f.slot(1, SLOTS), slice(g * HALF, (g + 1) * HALF)
                pe.matmul(bank[:, :], wq_hi[:, :], hid_hi[:, s, half], start=True, stop=False)
                pe.matmul(bank[:, :], wq_hi[:, :], hid_lo[:, s, half], start=False, stop=False)
                pe.matmul(bank[:, :], wq_lo[:, :], hid_hi[:, s, half], start=False, stop=True).then_inc(q_done, 1)

            def project_u(f, g):
                if not f.has(0):
                    return
                if g == 0:
                    if f.has(1):
                        pe.wait_ge(split_done, f.count(2, 1, 1))
                    else:
                        pe.wait_ge(u_raw_done, f.count(2, 0, 0))
                else:
                    pe.wait_ge(u_raw_done, f.count(2, 0, 1))
                s = f.slot(0, SLOTS)
                for j in range(HB):
                    block_n = slice((g * HB + j) * P, (g * HB + j + 1) * P)
                    u = bank_b[:, j * P:(j + 1) * P]
                    pe.matmul(u, hid_hi[:, s, block_n], g_hi[:, :], start=True, stop=False)
                    pe.matmul(u, hid_hi[:, s, block_n], g_lo[:, :], start=False, stop=False)
                    mm = pe.matmul(u, hid_lo[:, s, block_n], g_hi[:, :], start=False, stop=True)
                mm.then_inc(u_done, 1)

            def transform(f, g):
                d = -2 if g else -1
                if not f.has(d):
                    return
                if g:
                    pe.wait_ge(relu_done, f.count(2, d, 1))
                elif f.has(1):
                    pe.wait_ge(split_done, f.count(2, 1, 2))
                elif f.has(-2):
                    pe.wait_ge(relu_done, f.count(2, -2, 2))
                s, half = f.slot(d, SLOTS), slice(g * HALF, (g + 1) * HALF)
                pe.matmul(bank_a[:, :], wt_hi[:, :], hid_hi[:, s, half], start=True, stop=False)
                pe.matmul(bank_a[:, :], wt_hi[:, :], hid_lo[:, s, half], start=False, stop=False)
                pe.matmul(bank_a[:, :], wt_lo[:, :], hid_hi[:, s, half], start=False, stop=False)
                pe.wait_ge(zt_done, f.count(T, d, (g + 1) * HB))
                for j in range(HB):
                    mm = pe.matmul(bank_a[:, j * P:(j + 1) * P], zt[:, f.slot(d, 2), g * HB + j, :], ident,
                                   start=False, stop=(j == HB - 1), is_transpose=True)
                mm.then_inc(t_done, 1)

            def frame(f):
                for k in range(T):
                    energies(f, k)
                    attend(f, k)
                    if k == 1:
                        transform(f, 1)
                    elif k == 2:
                        project_q(f, 0)
                    elif k == 3:
                        project_q(f, 1)
                    elif k == 4:
                        project_u(f, 0)
                    elif k == 5:
                        transform(f, 0)
                    elif k == 6:
                        project_u(f, 1)

            frames(pe, frame)

        @block.vector
        def _(dve):
            steps = [0]

            def step(ins):
                steps[0] += 1
                ins.then_inc(setup_dve, 1)
                dve.wait_ge(setup_dve, steps[0])

            def stats(f):
                if not f.has(2):
                    return
                s = f.slot(2, SLOTS)
                dve.wait_ge(x_in[s], f.turn(2) * 16)
                for g in range(2):
                    dve.bn_stats(stat[:, g, :], x_sb[:, s, g * HALF:(g + 1) * HALF]).then_inc(stat_step, 1)

            def await_stats(f):
                if not f.has(2):
                    return
                dve.wait_ge(stat_step, f.count(2, 2, 2))
                if f.has(1):
                    dve.wait_ge(norm_done, f.count(1, 2, 0))

            def aggregate(f):
                if not f.has(2):
                    return
                dve.bn_aggr(mv[:, :], stat[:, :, :]).then_inc(stats_done, 1)

            before = Frame(-2, 0, B, SLOTS)
            stats(before)
            await_stats(before)
            aggregate(before)

            dve.wait_ge(weights_in, 16 * WEIGHTS)
            step(dve.tensor_reduce(absmax[:, 0:1], wv_sb[:, :], AX.X, ALU.max, apply_absolute_value=True))
            step(dve.tensor_reduce(absmax[:, 1:2], wq_sb[:, :], AX.X, ALU.max, apply_absolute_value=True))
            dve.wait_ge(setup_pool, MAX_DONE)
            step(dve.tensor_scalar(clipped[:, :], allmax[:, :], 2.0 ** -40, 2.0 ** 40, ALU.max, ALU.min))
            step(dve.tensor_scalar(pow2[:, :], clipped[:, :].bitcast(U32), EXPONENT_MASK, None, ALU.bitwise_and))
            step(dve.reciprocal(ipow2[:, :], pow2[:, :].bitcast(F32)))
            wt_pow2, wq_pow2 = (pow2[:, i:i + 1].bitcast(F32) for i in range(2))
            step(dve.tensor_scalar(lam[:, :], ipow2[:, 0:1], 2.0 ** 9, None, ALU.mult))
            step(dve.tensor_scalar(mu[:, :], ipow2[:, 0:1], 2.0 ** 4 / C, None, ALU.mult))
            step(dve.tensor_scalar(neg_mu[:, :], mu[:, :], -1.0, None, ALU.mult))
            step(dve.tensor_scalar(alpha[:, :], ipow2[:, 1:2], 2.0 ** 9 / C, None, ALU.mult))
            step(dve.tensor_scalar(beta[:, :], wq_pow2, wq_pow2, 2.0 ** -18 * C * C, ALU.mult, ALU.mult))
            step(dve.tensor_scalar(nbeta[:, :], beta[:, :], -1.0, None, ALU.mult))
            step(dve.tensor_scalar(wt_f32[:, :], wt_sb[:, :], lam[:, :], None, ALU.mult))
            step(dve.tensor_scalar(wq_f32[:, :], wq_sb[:, :], alpha[:, :], None, ALU.mult))
            step(dve.tensor_copy(wq_hi[:, :], wq_f32[:, :]))
            assert steps[0] == WT_DONE, steps
            step(dve.tensor_tensor(wq_lo[:, :], wq_f32[:, :], wq_hi[:, :], ALU.subtract))
            step(dve.tensor_copy(wt_hi[:, :], wt_f32[:, :]))
            step(dve.tensor_tensor(wt_lo[:, :], wt_f32[:, :], wt_hi[:, :], ALU.subtract))
            dve.wait_ge(setup_pool, BN_DONE)
            step(dve.tensor_scalar(t_scale[:, :], bn_scale[:, :], wt_pow2, 2.0 ** -9, ALU.mult, ALU.mult))
            dve.wait_ge(setup_pe, 2)
            step(dve.tensor_scalar(g_f32[:, :], bank_a[:, 0:P], mu[:, :], None, ALU.mult))
            step(dve.tensor_scalar(c_row[:, :], bank_b[:, 0:P], mu[:, :], None, ALU.mult))
            step(dve.tensor_copy(g_hi[:, :], g_f32[:, :]))
            step(dve.tensor_tensor(g_lo[:, :], g_f32[:, :], g_hi[:, :], ALU.subtract))
            assert steps[0] == DVE_READY, steps

            def row_max(f, k):
                if not f.has(0):
                    return
                dve.wait_ge(energy_done, f.count(T, 0, k + 1))
                dve.tensor_reduce(rowmax[:, k:k + 1], energy[k % 2][:, :], AX.X, ALU.max).then_inc(max_done, 1)
                dve.wait_ge(max_done, f.count(T, 0, k + 1))
                dve.tensor_scalar(nbias[:, k:k + 1], rowmax[:, k:k + 1], nbeta[:, :], None,
                                  ALU.mult).then_inc(nbias_done, 1)

            def invert_colsum(f, k):
                d, m = (-1, k - 3) if k >= 3 else (-2, T - 2)
                if k % 2 == 0 or not f.has(d):
                    return
                pair = m // 2 % 2
                colsum = zpsum[pair][:, 0:2 * W].rearrange("p (a w) -> p a w", w=W)[:, :, P:W]
                dve.wait_ge(z_done, f.count(T, d, m + 2))
                dve.tensor_scalar(den[:, pair, :, :], colsum, SOFT_EPS, neg_mu[:, :], ALU.add,
                                  ALU.mult).then_inc(den_done, 1)
                dve.wait_ge(den_done, f.count(HB, d, m // 2 + 1))
                dve.reciprocal(inv_den[:, pair, :, :], den[:, pair, :, :]).then_inc(inv_den_done, 1)

            def invert_rowsum(f, g):
                d = -1 if g else 0
                if not f.has(d):
                    return
                b, blocks = f.slot(d, 2), slice(g * HB, (g + 1) * HB)
                dve.wait_ge(prob_done, f.count(T, d, (g + 1) * HB))
                dve.reciprocal(ut[:, b, blocks, P:W], rowsum[:, b, blocks].rearrange("p (t a) -> p t a", a=1)
                               ).then_inc(inv_done, 1)

            def add_c(f, g):
                if not f.has(0):
                    return
                dve.wait_ge(u_done, f.count(2, 0, g + 1))
                if f.has(-1):
                    dve.wait_ge(ut_done, f.count(2, 0, g - 1))
                dve.tensor_tensor(u_raw[:, g * HB:(g + 1) * HB, :], bank_b[:, :].rearrange("p (t c) -> p t c", c=P),
                                  c_row[:, None, :].to_broadcast([P, HB, P]), ALU.add).then_inc(u_raw_done, 1)

            def split_q(f, g):
                if not f.has(1):
                    return
                b = f.slot(1, 2)
                half = slice(g * HALF, (g + 1) * HALF)
                bank = bank_a if g else bank_b
                dve.wait_ge(qhi_done, f.count(2, 1, g + 1))
                dve.scalar_tensor_tensor(q_mov[:, b, half], q_hi[:, half], mask_mov, bank[:, :], ALU.mult, ALU.add)
                dve.scalar_tensor_tensor(q_sta[:, b, half], q_hi[:, half], mask_sta, bank[:, :], ALU.mult,
                                         ALU.add).then_inc(split_done, 1)

            def frame(f):
                for k in range(T):
                    invert_colsum(f, k)
                    if k == 0:
                        invert_rowsum(f, 1)
                    elif k == 7:
                        await_stats(f)
                    row_max(f, k)
                    if k == 3:
                        split_q(f, 0)
                    elif k == 4:
                        split_q(f, 1)
                    elif k == 5:
                        add_c(f, 0)
                        invert_rowsum(f, 0)
                    elif k == 6:
                        stats(f)
                    elif k == 7:
                        aggregate(f)
                        add_c(f, 1)

            frames(dve, frame)

        @block.scalar
        def _(act):
            act.wait_ge(setup_pool, 2)
            act.activation(warm[:, :], zero[:, :], ACT.Exp)

            def softmax(f, k):
                if not f.has(0):
                    return
                if k == 0 and not f.looped and f.c == 0:
                    act.wait_ge(setup_dve, DVE_READY)
                if k == 0 and f.has(-2):
                    act.wait_ge(z_done, f.count(T, -1, 0))
                act.wait_ge(nbias_done, f.count(T, 0, k + 1))
                b = f.slot(0, 2)
                act.activation(prob[:, b, k, :], energy[k % 2][:, :], ACT.Exp, bias=nbias[:, k:k + 1],
                               scale=beta[:, :], accum_out=rowsum[:, b, k:k + 1]).then_inc(prob_done, 1)

            def hidden(f, high):
                if not f.has(1):
                    return
                s, b = f.slot(1, SLOTS), f.slot(1, 2)
                if high:
                    if f.has(-3):
                        act.wait_ge(t_done, f.count(2, -3, 2))
                else:
                    act.wait_ge(norm_done, f.count(1, 1, 1))
                act.activation(hid_hi[:, s, :] if high else hid[:, b, :], x_sb[:, s, :], ACT.Relu,
                               bias=norm[:, b, 1:2], scale=norm[:, b, 0:1]).then_inc(hid_done, 1)

            def high_q(f, g):
                if not f.has(1):
                    return
                half = slice(g * HALF, (g + 1) * HALF)
                act.wait_ge(q_done, f.count(2, 1, g + 1))
                if f.has(0):
                    act.wait_ge(split_done, f.count(2, 0, g + 1))
                act.activation(q_hi[:, half], (bank_a if g else bank_b)[:, :], ACT.Copy).then_inc(qhi_done, 1)

            def relu(f, g):
                d = -2 if g else -1
                if not f.has(d):
                    return
                act.wait_ge(t_done, f.count(2, d, g + 1))
                if f.has(d - 1):
                    act.wait_ge(y_done, f.count(2, d, g - 1))
                act.activation(act_t[:, g, :], bank_a[:, :], ACT.Relu, bias=bias[:, :],
                               scale=t_scale[:, :]).then_inc(relu_done, 1)

            def scale_z(f, k):
                d, m = (-1, k - 3) if k >= 3 else (-2, T - 2)
                if k % 2 == 0 or not f.has(d):
                    return
                pair = m // 2 % 2
                act.wait_ge(inv_den_done, f.count(HB, d, m // 2 + 1))
                if m == 0 and f.has(d - 2):
                    act.wait_ge(t_done, f.count(2, d, -2))
                for j in range(2):
                    act.activation(zt[:, f.slot(d, 2), m + j, :], zpsum[pair][:, j * W:j * W + P], ACT.Copy,
                                   scale=inv_den[:, pair, j, :]).then_inc(zt_done, 1)

            def frame(f):
                for k in range(T):
                    scale_z(f, k)
                    if k <= 1:
                        hidden(f, k == 1)
                    elif k == 2:
                        relu(f, 1)
                    elif k == 3:
                        high_q(f, 0)
                    elif k == 4:
                        high_q(f, 1)
                    elif k == 6:
                        relu(f, 0)
                    softmax(f, k)

            frames(act, frame)

        @block.gpsimd
        def _(pool):
            steps = [0]

            def step(ins):
                steps[0] += 1
                ins.then_inc(setup_pool, 1)
                pool.wait_ge(setup_pool, steps[0])

            def layer_norm(f):
                if not f.has(2):
                    return
                b = f.slot(2, 2)
                pool.wait_ge(stats_done, f.count(1, 2, 1))
                pool.tensor_tensor(veps[:, :], mv[:, 1:2], eps[:, :], ALU.add).then_inc(norm_step, 1)
                pool.wait_ge(norm_step, f.count(3, 2, 1))
                pool.tensor_tensor(norm[:, b, 0:1], veps[:, :], neg_half[:, 0:1], ALU.pow).then_inc(norm_step, 1)
                pool.wait_ge(norm_step, f.count(3, 2, 2))
                pool.tensor_tensor(mean_rstd[:, :], mv[:, 0:1], norm[:, b, 0:1], ALU.mult).then_inc(norm_step, 1)
                pool.wait_ge(norm_step, f.count(3, 2, 3))
                pool.tensor_tensor(norm[:, b, 1:2], zero[:, :], mean_rstd[:, :], ALU.subtract).then_inc(norm_done, 1)

            step(pool.memset(neg_half[:, :], -0.5))
            step(pool.memset(zero[:, :], 0.0))
            step(pool.memset(eps[:, :], NORM_EPS))
            layer_norm(Frame(-2, 0, B, SLOTS))
            pool.wait_ge(setup_dve, 2)
            step(pool.partition_all_reduce(allmax[:, :], absmax[:, :], P, bass.bass_isa.ReduceOp.max))
            assert steps[0] == MAX_DONE
            pool.wait_ge(weights_in, 16 * WEIGHTS)
            step(pool.tensor_tensor(bn_var[:, :], var_p, eps[:, :], ALU.add))
            step(pool.tensor_tensor(bn_inv[:, :], bn_var[:, :], neg_half[:, :], ALU.pow))
            step(pool.tensor_tensor(bn_scale[:, :], bn_inv[:, :], gamma_p, ALU.mult))
            step(pool.tensor_tensor(bias0[:, :], bt_p, mean_p, ALU.subtract))
            step(pool.tensor_tensor(bias1[:, :], bias0[:, :], bn_scale[:, :], ALU.mult))
            step(pool.tensor_tensor(bias[:, :], bias1[:, :], beta_p, ALU.add))
            assert steps[0] == BN_DONE

            def low_hidden(f):
                if not f.has(1):
                    return
                s = f.slot(1, SLOTS)
                pool.wait_ge(hid_done, f.count(2, 1, 2))
                for g in range(2):
                    half = slice(g * HALF, (g + 1) * HALF)
                    pool.tensor_tensor(hid_lo[:, s, half], hid[:, f.slot(1, 2), half], hid_hi[:, s, half],
                                       ALU.subtract).then_inc(hid_lo_done, 1)

            def add_hidden(f):
                if not f.has(1):
                    return
                s = f.slot(1, SLOTS)
                if f.has(-3):
                    pool.wait_ge(y_out[s], f.turn(-3) * 16)
                pool.tensor_tensor(xhy[:, s, :], x_sb[:, s, :], hid[:, f.slot(1, 2), :],
                                   ALU.add).then_inc(xh_done, 1)

            def scale_u(f, g):
                d = -1 if g else 0
                if not f.has(d):
                    return
                b, blocks = f.slot(d, 2), slice(g * HB, (g + 1) * HB)
                pool.wait_ge(inv_done, f.count(2, d, g + 1))
                pool.wait_ge(u_raw_done, f.count(2, d, g + 1))
                pool.tensor_tensor(ut[:, b, blocks, 0:P], u_raw[:, blocks, :],
                                   ut[:, b, blocks, P:W].to_broadcast([P, HB, P]), ALU.mult).then_inc(ut_done, 1)

            def finish(f, g):
                d = -2 if g else -1
                if not f.has(d):
                    return
                s = f.slot(d, SLOTS)
                half = slice(g * HALF, (g + 1) * HALF)
                pool.wait_ge(relu_done, f.count(2, d, g + 1))
                pool.wait_ge(xh_done, f.count(1, d, 1))
                pool.tensor_tensor(xhy[:, s, half], xhy[:, s, half], act_t[:, g, :], ALU.add).then_inc(y_done, 1)

            def frame(f):
                scale_u(f, 1)
                low_hidden(f)
                finish(f, 1)
                add_hidden(f)
                scale_u(f, 0)
                finish(f, 0)
                layer_norm(f)

            frames(pool, frame)


def kernel(x, adj, L0_gnn_wq, L0_gnn_bv, L0_gnn_bt, L0_gnn_gamma, L0_gnn_beta, L0_gnn_bn_mean, L0_gnn_bn_var):
    import concourse.bacc as _bacc
    from concourse.bass_utils import run_bass_kernel_spmd as _run

    P = 128
    x, adj, wq = np.asarray(x), np.asarray(adj), np.asarray(L0_gnn_wq)
    bv, bt = np.asarray(L0_gnn_bv), np.asarray(L0_gnn_bt)
    gamma, beta = np.asarray(L0_gnn_gamma), np.asarray(L0_gnn_beta)
    mean, var = np.asarray(L0_gnn_bn_mean), np.asarray(L0_gnn_bn_var)
    D, C = wq.shape

    consts = np.zeros((P, P + 2), np.float32)
    consts[:, 0:P] = np.eye(P, dtype=np.float32)
    group = np.arange(P) // D
    consts[:, P] = np.where(group >= 2, -1.0, 0.0)
    consts[:, P + 1] = np.where(group % 2 == 1, -1.0, 0.0)

    arrays = {
        "x": x,
        "adj": adj,
        "adj_t": np.ascontiguousarray(adj.T),
        "wq_t4": np.ascontiguousarray(np.concatenate([wq.T] * 4, axis=1)),
        "bv_rep": np.ascontiguousarray(np.broadcast_to(bv[:, None], (C, P))),
        "prm": np.stack([var, gamma, bt, mean, beta], axis=1),
        "consts": consts,
    }
    nc = _bacc.Bacc("TRN2", target_bir_lowering=False, num_devices=1)
    args = [nc.dram_tensor(f"in_{n}", a.shape, mybir.dt.from_np(a.dtype), kind="ExternalInput").ap()
            for n, a in arrays.items()]
    args.append(nc.dram_tensor("out_y", x.shape, mybir.dt.float32, kind="ExternalOutput").ap())
    gnn_block(nc, *args)
    r = _run(nc, [{f"in_{n}": a for n, a in arrays.items()}], core_ids=[0])
    return r.results[0]["out_y"]
```
